# Optimizing a Trainium2 kernel written in Bass

```python
import numpy as np
import jax
import jax.numpy as jnp

def _softmax(x, axis=-1):
    return jax.nn.softmax(x, axis=axis)

def _gelu(x):
    return jax.nn.gelu(x, approximate=True)

def _silu(x):
    return jax.nn.silu(x)

def _sigmoid(x):
    return jax.nn.sigmoid(x)

def _layernorm(x, axis=-1, eps=1e-05):
    m = jnp.mean(x, axis=axis, keepdims=True)
    v = jnp.var(x, axis=axis, keepdims=True)
    return (x - m) / jnp.sqrt(v + eps)

def _scatter_add(tgt, idx, src, axis=0):
    return tgt.at[idx].add(src)

def _segment_sum(src, seg, n):
    return jax.ops.segment_sum(src, seg, n)
kernel_name = 'mk_xattn_ffn_d1_seqx_r4_6e14e9'

def setup_inputs(seed: int=0):
    np.random.seed(seed)
    _w = jnp.asarray

    def _rec_inputs():
        import jax
        import jax.numpy as jnp
        _rk = jax.random.key(seed)
        x = -0.000125 + 0.9999 * jax.random.normal(jax.random.fold_in(_rk, 1), (4, 512, 512), jnp.float32)
        _lenS = 512 - jax.random.randint(jax.random.fold_in(_rk, 7), (4,), 0, max(1, 512 // 4) + 1, jnp.int32)
        _lenS2 = 512 - jax.random.randint(jax.random.fold_in(_rk, 8), (4,), 0, max(1, 512 // 4) + 1, jnp.int32)
        _ctx_2048P = jax.random.normal(jax.random.fold_in(_rk, 11), (4, 16, 512), jnp.float32)
        _ctx_2048c = jax.random.dirichlet(jax.random.fold_in(_rk, 511), 0.3 * jnp.ones((16,), jnp.float32), (4, 512))
        _ctx_2048t = jnp.einsum('bsk,bkd->bsd', _ctx_2048c, _ctx_2048P)
        _ctx_2048t = _ctx_2048t * jax.lax.rsqrt(jnp.mean(jnp.square(_ctx_2048t)) + 1e-12) * 0.953939
        ctx_2048 = -0.00010331 + 0.999899 * (_ctx_2048t + 0.3 * jax.random.normal(jax.random.fold_in(_rk, 611), (4, 512, 512), jnp.float32))
        _validS = jnp.arange(512)[None, :] < _lenS[:, None]
        _validS2 = jnp.arange(512)[None, :] < _lenS2[:, None]
        _causal = jnp.tril(jnp.ones((512, 512), dtype=bool))
        mask_Bx1xS2_ff0 = jnp.where(jnp.ones((4, 1, 512), dtype=bool), 0.0, -1000000000.0).astype(jnp.float32)
        return (x, ctx_2048, mask_Bx1xS2_ff0)
    x, ctx_2048, mask_Bx1xS2_ff0 = _rec_inputs()

    def _L0_xattn_setup():
        import jax, jax.numpy as jnp
        import numpy as np
        FP8_E4M3_MAX = 448.0
        EPS = 1e-12

        def _fp8_quant_dequant(x):
            amax = jnp.max(jnp.abs(x))
            scale = FP8_E4M3_MAX / jnp.maximum(amax, EPS)
            q = jnp.clip(x * scale, -FP8_E4M3_MAX, FP8_E4M3_MAX).astype(jnp.float8_e4m3fn)
            return q.astype(jnp.float32) / scale
        key = jax.random.key(seed)
        k1, k2 = jax.random.split(key)
        B, M, K, N = (32, 128, 512, 512)
        inp = jax.random.normal(k1, (B, M, K), dtype=jnp.float32)
        weight = jax.random.normal(k2, (B, K, N), dtype=jnp.float32)
        bias = jnp.zeros((B, 1, N), dtype=jnp.float32)
        return {'input': inp, 'weight': weight, 'bias': bias}
    _L0_xattn_all = _L0_xattn_setup()
    _L0_xattn_in = {k: v for k, v in _L0_xattn_all.items() if k in ()}
    del _L0_xattn_all

    def _L0_ffn_setup():
        import jax, jax.numpy as jnp
        import numpy as np
        L, B, D = (512, 1, 512)
        H = 16
        DK, DV = (D // 2, D)
        HDK, HDV = (DK // H, DV // H)
        RATIO = 2
        BASE = 10000.0
        EPS = 1e-05

        def _apply_rotary(x, cos, sin):
            d2 = x.shape[-1] // 2
            x1, x2 = (x[..., :d2], x[..., d2:])
            return jnp.concatenate([x1 * cos - x2 * sin, x2 * cos + x1 * sin], axis=-1)
        key = jax.random.key(seed)
        ks = jax.random.split(key, 8)
        s = 0.02
        return {'x': jax.random.normal(ks[0], (L, B, D), jnp.float32), 'conv_w': jax.random.normal(ks[1], (D, 2), jnp.float32) * 0.5, 'Wq': jax.random.normal(ks[2], (D, DK), jnp.float32) * s, 'Wk': jax.random.normal(ks[3], (D, DK), jnp.float32) * s, 'Wv': jax.random.normal(ks[4], (D, DV), jnp.float32) * s, 'Wg': jax.random.normal(ks[5], (D, DV), jnp.float32) * s, 'router_w': jax.random.normal(ks[6], (H, HDV, RATIO), jnp.float32) * s, 'Wout': jax.random.normal(ks[7], (DV, D), jnp.float32) * s}
    _L0_ffn_all = _L0_ffn_setup()
    _L0_ffn_in = {k: v for k, v in _L0_ffn_all.items() if k in ('conv_w', 'Wq', 'Wk', 'Wv', 'Wg', 'router_w', 'Wout')}
    del _L0_ffn_all
    return {'x': x, 'ctx_2048': ctx_2048, 'mask_Bx1xS2_ff0': mask_Bx1xS2_ff0, 'L0_ffn_conv_w': _L0_ffn_in['conv_w'], 'L0_ffn_Wq': _L0_ffn_in['Wq'], 'L0_ffn_Wk': _L0_ffn_in['Wk'], 'L0_ffn_Wv': _L0_ffn_in['Wv'], 'L0_ffn_Wg': _L0_ffn_in['Wg'], 'L0_ffn_router_w': _L0_ffn_in['router_w'], 'L0_ffn_Wout': _L0_ffn_in['Wout']}

def reference(x, ctx_2048, mask_Bx1xS2_ff0, L0_ffn_conv_w, L0_ffn_Wq, L0_ffn_Wk, L0_ffn_Wv, L0_ffn_Wg, L0_ffn_router_w, L0_ffn_Wout):
    import jax
    import jax.numpy as jnp

    def _L0_xattn_ref(input, weight, bias):
        import jax, jax.numpy as jnp
        import numpy as np
        FP8_E4M3_MAX = 448.0
        EPS = 1e-12

        def _fp8_quant_dequant(x):
            amax = jnp.max(jnp.abs(x))
            scale = FP8_E4M3_MAX / jnp.maximum(amax, EPS)
            q = jnp.clip(x * scale, -FP8_E4M3_MAX, FP8_E4M3_MAX).astype(jnp.float8_e4m3fn)
            return q.astype(jnp.float32) / scale
        x_dq = _fp8_quant_dequant(input)
        w_dq = _fp8_quant_dequant(weight)
        out = jnp.einsum('bmk,bkn->bmn', x_dq, w_dq)
        out = out + bias
        return out

    def _L0_ffn_ref(x, conv_w, Wq, Wk, Wv, Wg, router_w, Wout):
        import jax, jax.numpy as jnp
        import numpy as np
        L, B, D = (512, 1, 512)
        H = 16
        DK, DV = (D // 2, D)
        HDK, HDV = (DK // H, DV // H)
        RATIO = 2
        BASE = 10000.0
        EPS = 1e-05

        def _apply_rotary(x, cos, sin):
            d2 = x.shape[-1] // 2
            x1, x2 = (x[..., :d2], x[..., d2:])
            return jnp.concatenate([x1 * cos - x2 * sin, x2 * cos + x1 * sin], axis=-1)
        x = jnp.transpose(x, (1, 0, 2))
        b, l, d = x.shape
        x_prev = jnp.pad(x, ((0, 0), (1, 0), (0, 0)))[:, :l]
        x = jax.nn.silu(x_prev * conv_w[:, 0] + x * conv_w[:, 1])
        q = jax.nn.silu(x @ Wq)
        k = x @ Wk
        v = x @ Wv
        g = x @ Wg
        q = q.reshape(b, l, H, HDK).transpose(0, 2, 1, 3)
        k = k.reshape(b, l, H, HDK).transpose(0, 2, 1, 3)
        v = v.reshape(b, l, H, HDV).transpose(0, 2, 1, 3)
        inv_freq = 1.0 / BASE ** (jnp.arange(0, HDK, 2, dtype=jnp.float32) / HDK)
        freqs = jnp.arange(l, dtype=jnp.float32)[:, None] * inv_freq[None, :]
        cos, sin = (jnp.cos(freqs), jnp.sin(freqs))
        q = _apply_rotary(q, cos, sin)
        k = _apply_rotary(k, cos, sin)
        logits = jnp.einsum('bhld,hdr->bhlr', v, router_w)
        scores = jax.nn.softmax(logits, axis=-1)
        onehot = jax.nn.one_hot(jnp.argmax(scores, axis=-1), RATIO, dtype=scores.dtype)
        masked_scores = scores * onehot
        masked_ind = onehot
        sum_ind = jnp.cumsum(masked_ind, axis=2)
        norm = jnp.where(sum_ind > 0, 1.0 / jnp.maximum(sum_ind, 1.0), 0.0)[..., None]
        q_exp = q[:, :, :, None, :] * masked_scores[..., None] * norm
        k_exp = k[:, :, :, None, :] * masked_ind[..., None]
        q_exp = q_exp.reshape(b, H, l, RATIO * HDK)
        k_exp = k_exp.reshape(b, H, l, RATIO * HDK)
        qk = jnp.einsum('bhld,bhmd->bhlm', q_exp, k_exp) * HDK ** (-0.5)
        mask = jnp.tril(jnp.ones((l, l), dtype=qk.dtype))
        qk = qk * mask
        o = jnp.einsum('bhlm,bhmd->bhld', qk, v)
        o = o.transpose(0, 2, 1, 3)
        mu = jnp.mean(o, axis=-1, keepdims=True)
        var = jnp.var(o, axis=-1, keepdims=True)
        o = (o - mu) / jnp.sqrt(var + EPS)
        out = jax.nn.silu(g) * o.reshape(b, l, d)
        out = out @ Wout
        return jnp.transpose(out, (1, 0, 2))
    x = x + _L0_xattn_ref(_layernorm(x, axis=-1), ctx_2048, mask_Bx1xS2_ff0)
    x = x + _L0_ffn_ref(_layernorm(x, axis=-1), L0_ffn_conv_w, L0_ffn_Wq, L0_ffn_Wk, L0_ffn_Wv, L0_ffn_Wg, L0_ffn_router_w, L0_ffn_Wout)
    return x

_drawn_inputs = setup_inputs


def setup_inputs(seed=0):
    import zlib

    import numpy as np

    out = dict(_drawn_inputs(seed))
    spreads = {}
    factors = {'L0_ffn_conv_w': 8.0,
     'L0_ffn_Wq': 8.0,
     'L0_ffn_Wk': 8.0,
     'L0_ffn_Wv': 8.0,
     'L0_ffn_Wg': 8.0,
     'L0_ffn_router_w': 8.0,
     'L0_ffn_Wout': 8.0}
    for name, (base, spread) in spreads.items():
        noise = np.random.default_rng([zlib.crc32(name.encode()), seed]).standard_normal(out[name].shape)
        drawn = base * np.exp(spread * noise) if base else spread * noise
        out[name] = jnp.asarray(drawn.astype(out[name].dtype))
    for name, factor in factors.items():
        out[name] = (out[name] * factor).astype(out[name].dtype)
    return out
```

```python
import numpy as np
import concourse.bass as bass
from concourse import mybir
from concourse.alu_op_type import AluOpType as ALU
from contextlib import ExitStack


def xattn_ffn_kernel(nc: bass.Bass, x, ctx, mask, conv_w, Wq, Wk, Wv, Wg, router_w, Wout,
                     c_ident, c_rope, c_tril, out):
    fp32 = mybir.dt.float32
    f32r = mybir.dt.float32r
    bf16 = mybir.dt.bfloat16
    u32 = mybir.dt.uint32
    ACT = mybir.ActivationFunctionType
    AX = mybir.AxisListType.X

    P = 128
    L, S, D = x.shape
    T = S // P
    K = D // P
    H = router_w.shape[0]
    DK = Wq.shape[1]
    HDK = DK // H
    HDV = D // H
    NI = T * L
    FP8_MAX, FP8_EPS, LN_EPS = 448.0, 1e-12, 1e-5
    UP = 2.0 ** 20
    LEAST_MAGIC = 1.5 * 2.0 ** -6 * UP
    EXP_BITS, HALF_BIT = 0x7F800000, 0x00400000

    with ExitStack() as es:
        def sb(name, shape, dt=fp32):
            return es.enter_context(nc.sbuf_tensor(name, shape, dt))

        def sem(name):
            return es.enter_context(nc.semaphore(name))

        X = sb("X", [P, NI, D])
        CQ = sb("CQ", [P, L * K, D], bf16)
        Wqk_h, Wqk_l = sb("Wqk_h", [P, K, 2 * DK], f32r), sb("Wqk_l", [P, K, 2 * DK], f32r)
        Wv_h, Wv_l = sb("Wv_h", [P, K, D], f32r), sb("Wv_l", [P, K, D], f32r)
        Wg_h, Wg_l = sb("Wg_h", [P, K, D], f32r), sb("Wg_l", [P, K, D], f32r)
        Wo_h, Wo_l = sb("Wo_h", [P, K, D], f32r), sb("Wo_l", [P, K, D], f32r)
        Wr_h, Wr_l = sb("Wr_h", [P, K, H], f32r), sb("Wr_l", [P, K, H], f32r)
        stage = sb("stage", [P, 4, D])
        xq = sb("xq", [P, 2, D], bf16)
        xqT = sb("xqT", [P, 2, K, P], bf16)
        qk = sb("qk", [P, L, 2 * DK])
        v = sb("v", [P, L, D])
        o = sb("o", [P, L, D])
        cv = sb("cv", [P, 2, D])
        msk = sb("msk", [P, L, D])
        ident = sb("ident", [P, P])
        ident16 = sb("ident16", [P, P], bf16)
        rope = sb("rope", [P, 2, L, HDK])
        tril = sb("tril", [P, L * L])
        cw = sb("cw", [P, K, 2])
        ones2 = sb("ones2", [2, P])
        bst = sb("bst", [P, L, 6])
        mv = sb("mv", [P, L, 2])
        nmean = sb("nmean", [P, NI])
        ve = sb("ve", [P, NI])
        rstd = sb("rstd", [P, NI])
        mhalf = sb("mhalf", [P, L * H])
        xam = sb("xam", [P, NI])
        cam = sb("cam", [P, L])
        am2 = sb("am2", [P, 2])
        g2 = sb("g2", [2, 4])
        sc = sb("sc", [P, 8])
        rs, nb = sb("rs", [P, 2, NI]), sb("nb", [P, 2, NI])
        ln2 = sb("ln2", [P, 3, L])
        dif = sb("dif", [P, 5, L * H])
        pairs = sb("pairs", [P, 2, L, L, H])
        same, dots = pairs[:, 0, :, :, :], pairs[:, 1, :, :, :]
        wvm = sb("wvm", [P, K * H])
        ssq = sb("ssq", [P, 2, L * H])

        early = ExitStack()
        craw = early.enter_context(nc.sbuf_tensor("craw", [P, L, K, D], fp32))
        woraw = early.enter_context(nc.sbuf_tensor("woraw", [P, K, D], fp32))
        early.close()
        yh, yl = sb("yh", [P, K, L * P], f32r), sb("yl", [P, K, L * P], f32r)
        zh, zl = sb("zh", [P, K, L * P], f32r), sb("zl", [P, K, L * P], f32r)
        sg = sb("sg", [P, D])
        prod = sb("prod", [P, 2 * D])
        rot = sb("rot", [P, 2 * DK])

        rw = cv[:, :, :].rearrange("p a n -> p (a n)").rearrange("p (n r) -> p n r", r=2)
        rwd = pairs[:, :, :, :, :].rearrange("p a l m h -> p (a l m h)")
        wprod = xqT[:, :, :, :].rearrange("p a k n -> p (a k n)").bitcast(fp32)

        psT = [es.enter_context(nc.psum_tensor(f"psT{i}", [P, D], fp32)) for i in range(2)]
        psO = [es.enter_context(nc.psum_tensor(f"psO{i}", [P, D], fp32)) for i in range(2)]
        psC = [es.enter_context(nc.psum_tensor(f"psC{i}", [P, D], fp32)) for i in range(3)]
        psD = es.enter_context(nc.psum_tensor("psD", [P, D], fp32))

        s_x = [sem(f"s_xin{t}") for t in range(T)]
        s_c = [sem(f"s_cin{l}") for l in range(L)]
        s_small = sem("s_small")
        s_mask = sem("s_mask")
        s_id16 = sem("s_id16")
        s_w = [sem(f"s_win{i}") for i in range(4)]
        s_store = sem("s_store")
        s_dve = sem("s_dve")
        s_pool = sem("s_pool")
        s_act = sem("s_act")
        s_const = sem("s_const")
        s_stat = sem("s_stat")
        s_xc = sem("s_xc")
        s_xam = sem("s_xam")
        s_rstd = sem("s_rstd")
        s_am = sem("s_am")
        s_amT = sem("s_amT")
        s_diag = sem("s_diag")
        s_amB = sem("s_amB")
        s_scale = sem("s_scale")
        s_xs = sem("s_xs")
        s_q = sem("s_q")
        s_rwd = sem("s_rwd")
        s_wp = sem("s_wp")
        s_wpr = sem("s_wpr")
        s_wvm = sem("s_wvm")
        s_wvc = sem("s_wvc")
        s_whi = sem("s_whi")
        s_wlo = sem("s_wlo")
        s_wrh = sem("s_wrh")
        s_wrl = sem("s_wrl")
        s_AT = sem("s_AT")
        s_xqT = sem("s_xqT")
        s_AO = sem("s_AO")
        s_xm = sem("s_xm")
        s_x1 = sem("s_x1")
        s_ln2 = sem("s_ln2")
        s_rstd1 = sem("s_rstd1")
        s_nb1 = sem("s_nb1")
        s_xn2 = sem("s_xn2")
        s_BT = sem("s_BT")
        s_cm = sem("s_cm")
        s_cv = sem("s_cv")
        s_y = sem("s_y")
        s_yh = sem("s_yh")
        s_yl = sem("s_yl")
        s_C = sem("s_C")
        s_Cev = sem("s_Cev")
        s_R = sem("s_R")
        s_dif = sem("s_dif")
        s_th = sem("s_th")
        s_rot = sem("s_rot")
        s_co = sem("s_co")
        s_o = sem("s_o")
        s_op = sem("s_op")
        s_sq = sem("s_sq")
        s_ssqr = sem("s_ssqr")
        s_ssq = sem("s_ssq")
        s_rstdo = sem("s_rstdo")
        s_on = sem("s_on")
        s_z = sem("s_z")
        s_DT = sem("s_DT")
        s_zh = sem("s_zh")
        s_zl = sem("s_zl")
        s_EO = sem("s_EO")
        s_out = sem("s_out")

        block = es.enter_context(nc.Block())
        CHUNKS = 3
        JOBS = CHUNKS * L

        @block.sync
        def _(sp):
            for t in range(T):
                sp.dma_start(X[:, t * L:(t + 1) * L, :],
                             x[:, t * P:(t + 1) * P, :].rearrange("l p d -> p l d")).then_inc(s_x[t], 16)
            for l in range(L):
                sp.dma_start(craw[:, l, :, :], ctx[l, :, :].rearrange("(k p) n -> p k n", p=P)).then_inc(s_c[l], 16)
            sp.dma_start(msk[:, :, :], mask.rearrange("l o n -> o l n").broadcast_to([P, L, D])).then_inc(s_mask, 16)
            sp.dma_start(v[:, :, :], Wv.rearrange("(k p) n -> p k n", p=P)).then_inc(s_w[1], 16)
            sp.dma_start(qk[:, :, 0:DK], Wq.rearrange("(k p) n -> p k n", p=P)).then_inc(s_w[0], 16)
            sp.dma_start(qk[:, :, DK:2 * DK], Wk.rearrange("(k p) n -> p k n", p=P)).then_inc(s_w[0], 16)
            sp.dma_start(o[:, :, :], Wg.rearrange("(k p) n -> p k n", p=P)).then_inc(s_w[2], 16)
            sp.dma_start(woraw[:, :, :], Wout.rearrange("(k p) n -> p k n", p=P)).then_inc(s_w[3], 16)
            for t in range(T):
                for l in range(L):
                    sp.wait_ge(s_out, t * L + l + 1)
                    sp.dma_start(out[l, t * P:(t + 1) * P, :], X[:, t * L + l, :]).then_inc(s_store, 16)
            sp.wait_ge(s_store, 16 * NI)

        @block.scalar
        def _(act):
            act.dma_start(ident[:, :], c_ident).then_inc(s_small, 16)
            act.dma_start(rope[:, :, :, :], c_rope.broadcast_to([P, 2, L, HDK])).then_inc(s_small, 16)
            act.dma_start(tril[:, :], c_tril.broadcast_to([P, L * L])).then_inc(s_small, 16)
            act.dma_start(cw[:, :, :], conv_w.rearrange("(k p) j -> p k j", p=P)).then_inc(s_small, 16)
            act.dma_start(rw, router_w.rearrange("h d r -> (h d) r").unsqueeze(0).broadcast_to([P, D, 2])).then_inc(s_small, 16)

            for i in range(NI):
                act.wait_ge(s_stat, i // L + 1)
                if i >= 4:
                    act.wait_ge(s_xam, i - 3)
                nc.scalar.activation(stage[:, i % 4, :], X[:, i, :], ACT.Identity,
                                     bias=nmean[:, i:i + 1]).then_inc(s_xc, 1)

            def scaled(n, src, a, b, a_up, b_up):
                if n >= 2:
                    act.wait_ge(s_q, n - 1)
                nc.scalar.activation(stage[:, n % 2, :], src, ACT.Identity, bias=b, scale=a)
                nc.scalar.activation(stage[:, 2 + n % 2, :], src, ACT.Identity, bias=b_up, scale=a_up).then_inc(s_xs, 1)

            act.wait_ge(s_scale, 1)
            for n in range(L * K):
                scaled(n, craw[:, n // K, n % K, :], sc[:, 3:4], 0.0, sc[:, 4:5], 0.0)

            def x_scaled(t, l):
                if t >= 1 and l == 0:
                    act.wait_ge(s_BT, t * K)
                i = t * L + l
                scaled(L * K + i, X[:, i, :], rs[:, 0, i:i + 1], nb[:, 0, i:i + 1],
                       rs[:, 1, i:i + 1], nb[:, 1, i:i + 1])

            def a_evac(t, l):
                n = t * L + l
                act.wait_ge(s_AT, n + 1)
                if n >= 2:
                    act.wait_ge(s_AO, n - 1)
                else:
                    act.wait_ge(s_wpr, K)
                nc.scalar.activation(xqT[:, n % 2, :, :],
                                     psT[n % 2][:, 0:K * P // 2].bitcast(bf16).rearrange("p (k n) -> p k n", k=K),
                                     ACT.Copy).then_inc(s_xqT, 1)

            def xn2(t, l):
                if l == 0:
                    act.wait_ge(s_q, L * K + (t + 1) * L)
                    act.wait_ge(s_nb1, t + 1)
                nc.scalar.activation(stage[:, l, :], X[:, t * L + l, :], ACT.Identity,
                                     bias=ln2[:, 2, l:l + 1], scale=ln2[:, 1, l:l + 1]).then_inc(s_xn2, 1)

            def conv(t, k):
                n = t * K + k
                act.wait_ge(s_BT, n + 1)
                if n >= 2:
                    act.wait_ge(s_yl, n - 1)
                if t >= 1:
                    act.wait_ge(s_ssqr, t * L)
                nc.scalar.activation(cv[:, n % 2, :], psT[k % 2][:, :], ACT.Identity,
                                     scale=cw[:, k, 1:2]).then_inc(s_cm, 1)
                act.wait_ge(s_cv, n + 1)
                nc.scalar.activation(cv[:, n % 2, :], cv[:, n % 2, :], ACT.Silu).then_inc(s_y, 1)
                act.wait_ge(s_y, n + 1)
                if k == 0 and t >= 1:
                    act.wait_ge(s_C, t * JOBS)
                nc.scalar.activation(yh[:, k, :], cv[:, n % 2, :], ACT.Copy).then_inc(s_yh, 1)

            def w_hi(n, dst, src):
                nc.scalar.activation(dst, src, ACT.Copy).then_inc(s_whi, 1)

            for l in range(L):
                x_scaled(0, l)
            for l in range(L):
                a_evac(0, l)
            act.wait_ge(s_w[0], 32)
            w_hi(0, Wqk_h[:, :, :], qk[:, :, :])
            for l in range(L):
                xn2(0, l)
            act.wait_ge(s_wvc, 1)
            w_hi(1, Wv_h[:, :, :], v[:, :, :])
            for k in range(K):
                conv(0, k)
            act.wait_ge(s_wpr, K)
            nc.scalar.activation(Wr_h[:, :, :], dif[:, 0, :].rearrange("p (k h) -> p k h", k=K), ACT.Copy).then_inc(s_wrh, 1)
            act.wait_ge(s_w[2], 16)
            w_hi(2, Wg_h[:, :, :], o[:, :, :])
            act.wait_ge(s_w[3], 16)
            w_hi(3, Wo_h[:, :, :], woraw[:, :, :])

            def c_wait(t, c, l):
                act.wait_ge(s_C, t * JOBS + c * L + l + 1)
                return psC[(c * L + l) % 3]

            for t in range(T):
                last = t == T - 1
                for l in range(L):
                    bank = c_wait(t, 0, l)
                    if t == 0:
                        act.wait_ge(s_wlo, 1)
                    else:
                        act.wait_ge(s_co, t)
                    nc.scalar.activation(qk[:, l, 0:DK], bank[:, 0:DK], ACT.Silu)
                    nc.scalar.activation(qk[:, l, DK:], bank[:, DK:2 * DK], ACT.Copy).then_inc(s_Cev, 1)
                    if not last:
                        x_scaled(t + 1, l)
                if not last:
                    for l in range(L):
                        a_evac(t + 1, l)
                for l in range(L):
                    bank = c_wait(t, 1, l)
                    if t == 0:
                        act.wait_ge(s_wlo, 2)
                    nc.scalar.activation(v[:, l, :], bank[:, :], ACT.Copy).then_inc(s_Cev, 1)
                act.wait_ge(s_dif, t + 1)
                nc.scalar.activation(dif[:, 2, :], dif[:, 1, :], ACT.Tanh, scale=0.5).then_inc(s_th, 1)
                if not last:
                    for l in range(L):
                        xn2(t + 1, l)

                def square(l):
                    n = t * L + l
                    act.wait_ge(s_op if l < 2 else s_o, t * 2 + l % 2 + 1)
                    if n >= 2:
                        act.wait_ge(s_ssqr, n - 1)
                    if t == 0 and l == 0:
                        act.wait_ge(s_yl, K)
                    if t >= 1 and l == 0:
                        act.wait_ge(s_yl, (t + 1) * K)
                    nc.scalar.activation(cv[:, n % 2, :], o[:, l, :], ACT.Square).then_inc(s_sq, 1)

                def gate(l):
                    n = t * L + l
                    bank = c_wait(t, 2, l)
                    if n >= 1:
                        act.wait_ge(s_z, n)
                    if t == 0 and l == 0:
                        act.wait_ge(s_wlo, 4)
                    nc.scalar.activation(sg[:, :], bank[:, :], ACT.Silu).then_inc(s_Cev, 1)

                square(0)
                square(1)
                gate(0)
                square(2)
                square(3)
                for l in range(1, L):
                    gate(l)
                if not last:
                    for k in range(K):
                        conv(t + 1, k)
                for k in range(K):
                    act.wait_ge(s_DT, t * K + k + 1)
                    if k == 0 and t >= 1:
                        act.wait_ge(s_EO, t * L)
                    nc.scalar.activation(zh[:, k, :], psT[k % 2][:, :], ACT.Copy).then_inc(s_zh, 1)

        @block.vector
        def _(dve):
            chain = [0]

            def link(ins):
                chain[0] += 1
                ins.then_inc(s_dve, 1)
                dve.wait_ge(s_dve, chain[0])

            nc.vector.memset(ones2[:, :], 1.0)
            nc.vector.memset(mhalf[:, :], -0.5).then_inc(s_const, 1)

            def stats(i, src):
                for l in range(L):
                    ins = nc.vector.bn_stats(bst[:, l, :], src[:, l, :])
                link(ins)
                for l in range(L):
                    ins = nc.vector.bn_aggr(mv[:, l, :], bst[:, l, :])
                link(ins)

            def x_max(i):
                dve.wait_ge(s_xc, i + 1)
                nc.vector.tensor_reduce(xam[:, i:i + 1], stage[:, i % 4, :], AX, ALU.max,
                                        apply_absolute_value=True).then_inc(s_xam, 1)

            for t in range(T):
                dve.wait_ge(s_x[t], 16)
                stats(t, X[:, t * L:(t + 1) * L, :])
                nc.vector.tensor_scalar(ve[:, t * L:(t + 1) * L], mv[:, :, 1], LN_EPS, None, ALU.add)
                nc.vector.tensor_scalar(nmean[:, t * L:(t + 1) * L], mv[:, :, 0], -1.0, None, ALU.mult).then_inc(s_stat, 1)
                if t >= 1:
                    for l in range(L):
                        x_max((t - 1) * L + l)
            for l in range(L):
                x_max((T - 1) * L + l)
            for l in range(L):
                dve.wait_ge(s_c[l], 16)
                ins = nc.vector.tensor_reduce(cam[:, l:l + 1], craw[:, l, :, :].rearrange("p k n -> p (k n)"),
                                              AX, ALU.max, apply_absolute_value=True)
            dve.wait_ge(s_rstd, T)
            dve.wait_ge(s_xam, NI)
            link(ins)
            link(nc.vector.tensor_tensor(xam[:, :], xam[:, :], rstd[:, :], ALU.mult))
            nc.vector.tensor_reduce(am2[:, 1:2], cam[:, :], AX, ALU.max)
            nc.vector.tensor_reduce(am2[:, 0:1], xam[:, :], AX, ALU.max).then_inc(s_am, 1)
            dve.wait_ge(s_amT, 1)
            link(nc.vector.tensor_reduce(g2[:, 0:1], psD[0:2, 0:P], AX, ALU.max))
            link(nc.vector.tensor_scalar(g2[:, 1:2], g2[:, 0:1], FP8_EPS, None, ALU.max))
            dve.wait_ge(s_small, 16 * 5)
            nc.vector.tensor_scalar(g2[:, 2:4], ident[0:2, 0:2], g2[:, 1:2], None, ALU.mult).then_inc(s_diag, 1)
            dve.wait_ge(s_amB, 1)
            link(nc.vector.tensor_copy(sc[:, 0:2], psD[:, 0:2]))
            nc.vector.tensor_scalar(sc[:, 5:6], sc[:, 0:1], sc[:, 1:2], FP8_MAX ** -2, ALU.mult, ALU.mult)
            link(nc.vector.reciprocal(sc[:, 6:8], sc[:, 0:2]))
            link(nc.vector.tensor_scalar(sc[:, 2:4], sc[:, 6:8], FP8_MAX, None, ALU.mult))
            nc.vector.tensor_scalar(sc[:, 4:5], sc[:, 3:4], UP, None, ALU.mult)
            link(nc.vector.tensor_scalar(rs[:, 0, :], rstd[:, :], sc[:, 2:3], None, ALU.mult))
            link(nc.vector.tensor_tensor(nb[:, 0, :], nmean[:, :], rs[:, 0, :], ALU.mult))
            nc.vector.tensor_scalar(rs[:, 1, :], rs[:, 0, :], UP, None, ALU.mult)
            nc.vector.tensor_scalar(nb[:, 1, :], nb[:, 0, :], UP, None, ALU.mult).then_inc(s_scale, 1)

            def quantise(n, dst):
                val, mag = stage[:, n % 2, :], stage[:, 2 + n % 2, :]
                dve.wait_ge(s_xs, n + 1)
                bits = mag.bitcast(u32)
                link(nc.vector.tensor_scalar(bits, bits, EXP_BITS, HALF_BIT, ALU.bitwise_and, ALU.bitwise_or))
                link(nc.vector.scalar_tensor_tensor(out=val, in0=mag, scalar=LEAST_MAGIC, in1=val,
                                                    op0=ALU.max, op1=ALU.add))
                nc.vector.scalar_tensor_tensor(out=dst, in0=mag, scalar=LEAST_MAGIC, in1=val, op0=ALU.max,
                                               op1=ALU.subtract, reverse1=True).then_inc(s_q, 1)

            def x_quantise(t, l):
                i = t * L + l
                if i >= 2:
                    dve.wait_ge(s_AT, i - 1)
                quantise(L * K + i, xq[:, i % 2, :])

            def x1(t, l):
                i = t * L + l
                dve.wait_ge(s_AO, i + 1)
                dve.wait_ge(s_xm, i + 1)
                nc.vector.scalar_tensor_tensor(out=X[:, i, :], in0=psO[i % 2][:, :], scalar=sc[:, 5:6],
                                               in1=X[:, i, :], op0=ALU.mult, op1=ALU.add).then_inc(s_x1, 1)

            def x1_stats(t):
                dve.wait_ge(s_x1, (t + 1) * L)
                if t >= 1:
                    dve.wait_ge(s_xn2, t * L)
                stats(t, X[:, t * L:(t + 1) * L, :])
                nc.vector.tensor_scalar(ln2[:, 0, :], mv[:, :, 1], LN_EPS, None, ALU.add).then_inc(s_ln2, 1)
                dve.wait_ge(s_rstd1, t + 1)
                nc.vector.scalar_tensor_tensor(out=ln2[:, 2, :], in0=mv[:, :, 0], scalar=-1.0, in1=ln2[:, 1, :],
                                               op0=ALU.mult, op1=ALU.mult).then_inc(s_nb1, 1)

            def conv(t, k):
                n = t * K + k
                dve.wait_ge(s_cm, n + 1)
                nc.vector.scalar_tensor_tensor(out=cv[:, n % 2, P:], in0=psT[k % 2][:, 0:(L - 1) * P],
                                               scalar=cw[:, k, 0:1], in1=cv[:, n % 2, P:],
                                               op0=ALU.mult, op1=ALU.add).then_inc(s_cv, 1)

            nc.vector.tensor_tensor(rwd, rw[:, :, 0], rw[:, :, 1], ALU.subtract).then_inc(s_rwd, 1)
            for n in range(L * K):
                quantise(n, CQ[:, n, :])
                if n >= (L - 1) * K:
                    k = n - (L - 1) * K
                    dve.wait_ge(s_wp, k + 1)
                    nc.vector.tensor_reduce(dif[:, 0, k * H:(k + 1) * H], wprod.rearrange("p (h d) -> p h d", h=H),
                                            AX, ALU.add).then_inc(s_wpr, 1)
            for l in range(L):
                x_quantise(0, l)
            dve.wait_ge(s_w[1], 16)
            link(nc.vector.tensor_reduce(wvm[:, :], v[:, :, :].rearrange("p k (h d) -> p (k h) d", h=H), AX, ALU.add))
            nc.vector.tensor_scalar(wvm[:, :], wvm[:, :], 1.0 / HDV, None, ALU.mult).then_inc(s_wvm, 1)
            for l in range(L):
                x1(0, l)
            x1_stats(0)
            for k in range(K):
                conv(0, k)
            dve.wait_ge(s_wp, K)
            nc.vector.memset(dots, 0.0)

            def dot(t, l):
                dve.wait_ge(s_rot, t * (L - 1) + max(l, 1))
                n = (l + 1) * DK
                link(nc.vector.tensor_tensor(
                    prod[:, 0:n].rearrange("p (m c) -> p m c", m=l + 1),
                    qk[:, l, 0:DK].unsqueeze(1).broadcast_to([P, l + 1, DK]),
                    qk[:, 0:l + 1, DK:], ALU.mult))
                ins = nc.vector.tensor_reduce(dots[:, l, 0:l + 1, :].rearrange("p m h -> p (m h)"),
                                              prod[:, 0:n].rearrange("p (g d) -> p g d", d=HDK), AX, ALU.add)
                link(ins)

            for t in range(T):
                last = t == T - 1
                if not last:
                    for l in range(L):
                        x_quantise(t + 1, l)
                if t == 0:
                    dve.wait_ge(s_wlo, 4)
                dot(t, 0)
                dot(t, 1)
                if not last:
                    for l in range(L):
                        x1(t + 1, l)
                    x1_stats(t + 1)
                dve.wait_ge(s_R, t + 1)
                if t == 0:
                    dve.wait_ge(s_wrl, 1)
                link(nc.vector.tensor_copy(dif[:, 0, :], psD[:, 0:L * H]))
                nc.vector.scalar_tensor_tensor(out=dif[:, 1, :], in0=dif[:, 0, :], scalar=-1.0, in1=dif[:, 0, :],
                                               op0=ALU.mult, op1=ALU.max).then_inc(s_dif, 1)
                link(nc.vector.tensor_scalar(dif[:, 3, :], dif[:, 0, :], 0.0, None, ALU.is_lt))
                dot(t, 2)
                dot(t, 3)
                win = dif[:, 3, :].rearrange("p (l h) -> p l h", l=L)
                for l in range(L):
                    ins = nc.vector.tensor_tensor(same[:, l, :, :], win, win[:, l, :].unsqueeze(1).broadcast_to([P, L, H]),
                                                  ALU.is_equal)
                link(ins)
                link(nc.vector.tensor_tensor(same[:, :, :, :].rearrange("p l m h -> p (l m) h"),
                                             same[:, :, :, :].rearrange("p l m h -> p (l m) h"),
                                             tril[:, :].unsqueeze(2).broadcast_to([P, L * L, H]), ALU.mult))
                for l in range(L):
                    ins = nc.vector.tensor_reduce(dif[:, 4, l * H:(l + 1) * H],
                                                  same[:, l, :, :].rearrange("p m h -> p h m"), AX, ALU.add)
                link(ins)
                link(nc.vector.reciprocal(dif[:, 4, :], dif[:, 4, :]))
                dve.wait_ge(s_th, t + 1)
                half = 0.5 * HDK ** -0.5
                link(nc.vector.tensor_scalar(dif[:, 2, :], dif[:, 2, :], half, half, ALU.mult, ALU.add))
                link(nc.vector.tensor_tensor(dif[:, 4, :], dif[:, 4, :], dif[:, 2, :], ALU.mult))
                link(nc.vector.tensor_tensor(same[:, :, :, :], same[:, :, :, :], dots[:, :, :, :], ALU.mult))
                for l in range(L):
                    ins = nc.vector.tensor_tensor(same[:, l, :, :], same[:, l, :, :],
                                                  dif[:, 4, l * H:(l + 1) * H].unsqueeze(1).broadcast_to([P, L, H]), ALU.mult)
                ins.then_inc(s_co, 1)
                dve.wait_ge(s_co, t + 1)

                def weigh(dst, l, m):
                    return nc.vector.tensor_tensor(
                        dst.rearrange("p (h d) -> p h d", h=H), v[:, m, :].rearrange("p (h d) -> p h d", h=H),
                        same[:, l, m, :].unsqueeze(2).broadcast_to([P, H, HDV]), ALU.mult)

                if t == 0:
                    dve.wait_ge(s_wlo, 3)
                for l in (2, 3):
                    dve.wait_ge(s_Cev, t * JOBS + L + l + 1)
                    if l == 2 and t >= 1:
                        dve.wait_ge(s_DT, t * K)
                    weigh(o[:, l, :], l, 0)
                    link(weigh(prod[:, 0:D], l, 1))
                    nc.vector.tensor_tensor(o[:, l, :], o[:, l, :], prod[:, 0:D], ALU.add)
                    link(weigh(prod[:, D:2 * D], l, 2))
                    if l == 3:
                        nc.vector.tensor_tensor(o[:, l, :], o[:, l, :], prod[:, D:2 * D], ALU.add)
                        link(weigh(prod[:, 0:D], l, 3))
                        nc.vector.tensor_tensor(o[:, l, :], o[:, l, :], prod[:, 0:D], ALU.add).then_inc(s_o, 1)
                    else:
                        nc.vector.tensor_tensor(o[:, l, :], o[:, l, :], prod[:, D:2 * D], ALU.add).then_inc(s_o, 1)
                for l in range(L):
                    n = t * L + l
                    dve.wait_ge(s_sq, n + 1)
                    nc.vector.tensor_reduce(ssq[:, 0, l * H:(l + 1) * H],
                                            cv[:, n % 2, :].rearrange("p (h d) -> p h d", h=H), AX, ALU.add).then_inc(s_ssqr, 1)
                dve.wait_ge(s_ssqr, (t + 1) * L)
                nc.vector.tensor_scalar(ssq[:, 0, :], ssq[:, 0, :], 1.0 / HDV, LN_EPS, ALU.mult, ALU.add).then_inc(s_ssq, 1)
                for l in range(L):
                    n = t * L + l
                    dve.wait_ge(s_on, n + 1)
                    dve.wait_ge(s_Cev, t * JOBS + 2 * L + l + 1)
                    nc.vector.tensor_tensor(o[:, l, :], o[:, l, :], sg[:, :], ALU.mult).then_inc(s_z, 1)
                if not last:
                    for k in range(K):
                        conv(t + 1, k)
                for k in range(K):
                    dve.wait_ge(s_zh, t * K + k + 1)
                    if k == 0 and t >= 1:
                        dve.wait_ge(s_EO, t * L)
                    nc.vector.tensor_tensor(zl[:, k, :], psT[k % 2][:, :], zh[:, k, :].bitcast(fp32), ALU.subtract).then_inc(s_zl, 1)
                for l in range(L):
                    i = t * L + l
                    dve.wait_ge(s_EO, i + 1)
                    nc.vector.tensor_tensor(X[:, i, :], psO[i % 2][:, :], X[:, i, :], ALU.add).then_inc(s_out, 1)

        @block.gpsimd
        def _(pool):
            chain = [0]

            def link(ins):
                chain[0] += 1
                ins.then_inc(s_pool, 1)
                pool.wait_ge(s_pool, chain[0])

            pool.wait_ge(s_small, 16 * 5)
            nc.gpsimd.tensor_copy(ident16[:, :], ident[:, :]).then_inc(s_id16, 1)
            pool.wait_ge(s_const, 1)
            for t in range(T):
                pool.wait_ge(s_stat, t + 1)
                nc.gpsimd.tensor_tensor(rstd[:, t * L:(t + 1) * L], ve[:, t * L:(t + 1) * L], mhalf[:, 0:L],
                                        ALU.pow).then_inc(s_rstd, 1)

            def w_lo(n, dst, src, hi):
                pool.wait_ge(s_whi, n + 1)
                nc.gpsimd.tensor_tensor(dst, src, hi.bitcast(fp32), ALU.subtract).then_inc(s_wlo, 1)

            pool.wait_ge(s_w[1], 16)
            pool.wait_ge(s_rwd, 1)
            for k in range(K):
                if k >= 1:
                    pool.wait_ge(s_wpr, k)
                nc.gpsimd.tensor_tensor(wprod, v[:, k, :], rwd, ALU.mult).then_inc(s_wp, 1)
            pool.wait_ge(s_wvm, 1)
            nc.gpsimd.tensor_tensor(v[:, :, :].rearrange("p k (h d) -> p (k h) d", h=H),
                                    v[:, :, :].rearrange("p k (h d) -> p (k h) d", h=H),
                                    wvm[:, :].unsqueeze(2).broadcast_to([P, K * H, HDV]), ALU.subtract).then_inc(s_wvc, 1)
            pool.wait_ge(s_mask, 16)
            for l in range(L):
                pool.wait_ge(s_xs, L * K + l + 1)
                nc.gpsimd.tensor_tensor(X[:, l, :], X[:, l, :], msk[:, l, :], ALU.add).then_inc(s_xm, 1)
            pool.wait_ge(s_ln2, 1)
            nc.gpsimd.tensor_tensor(ln2[:, 1, :], ln2[:, 0, :], mhalf[:, 0:L], ALU.pow).then_inc(s_rstd1, 1)
            w_lo(0, Wqk_l[:, :, :], qk[:, :, :], Wqk_h[:, :, :])

            def y_lo(t, k):
                n = t * K + k
                pool.wait_ge(s_yh, n + 1)
                if k == 0 and t >= 1:
                    pool.wait_ge(s_C, t * JOBS)
                nc.gpsimd.tensor_tensor(yl[:, k, :], cv[:, n % 2, :], yh[:, k, :].bitcast(fp32),
                                        ALU.subtract).then_inc(s_yl, 1)

            for k in range(K):
                y_lo(0, k)
            w_lo(1, Wv_l[:, :, :], v[:, :, :], Wv_h[:, :, :])
            pool.wait_ge(s_wrh, 1)
            nc.gpsimd.tensor_tensor(Wr_l[:, :, :], dif[:, 0, :].rearrange("p (k h) -> p k h", k=K),
                                    Wr_h[:, :, :].bitcast(fp32), ALU.subtract).then_inc(s_wrl, 1)
            w_lo(2, Wg_l[:, :, :], o[:, :, :], Wg_h[:, :, :])
            w_lo(3, Wo_l[:, :, :], woraw[:, :, :], Wo_h[:, :, :])
            pool.wait_ge(s_small, 16 * 5)
            pool.wait_ge(s_wlo, 4)

            def rotate(t, l):
                pool.wait_ge(s_Cev, t * JOBS + l + 1)
                half = HDK // 2
                n = 2 * H
                a = qk[:, l, :].rearrange("p (g j d) -> p g j d", g=n, j=2)
                r = rot[:, :].rearrange("p (g j d) -> p g j d", g=n, j=2)
                for j in range(2):
                    sin = rope[:, 1, l, j * half:(j + 1) * half].unsqueeze(1).broadcast_to([P, n, half])
                    ins = nc.gpsimd.tensor_tensor(r[:, :, j, :], a[:, :, 1 - j, :], sin, ALU.mult)
                link(ins)
                flat = qk[:, l, :].rearrange("p (g d) -> p g d", g=n)
                link(nc.gpsimd.tensor_tensor(flat, flat, rope[:, 0, l, :].unsqueeze(1).broadcast_to([P, n, HDK]), ALU.mult))
                nc.gpsimd.tensor_tensor(qk[:, l, :], qk[:, l, :], rot[:, :], ALU.add).then_inc(s_rot, 1)
                pool.wait_ge(s_rot, t * (L - 1) + l)

            def add_mask(t, l):
                i = t * L + l
                pool.wait_ge(s_xs, L * K + i + 1)
                nc.gpsimd.tensor_tensor(X[:, i, :], X[:, i, :], msk[:, l, :], ALU.add).then_inc(s_xm, 1)

            for t in range(T):
                last = t == T - 1
                for l in range(1, L):
                    rotate(t, l)
                    if not last:
                        add_mask(t + 1, l - 1)
                if not last:
                    add_mask(t + 1, L - 1)
                    pool.wait_ge(s_ln2, t + 2)
                    nc.gpsimd.tensor_tensor(ln2[:, 1, :], ln2[:, 0, :], mhalf[:, 0:L], ALU.pow).then_inc(s_rstd1, 1)
                pool.wait_ge(s_co, t + 1)
                if t >= 1:
                    pool.wait_ge(s_DT, t * K)

                def weigh(dst, l, m):
                    return nc.gpsimd.tensor_tensor(
                        dst.rearrange("p (h d) -> p h d", h=H), v[:, m, :].rearrange("p (h d) -> p h d", h=H),
                        same[:, l, m, :].unsqueeze(2).broadcast_to([P, H, HDV]), ALU.mult)

                pool.wait_ge(s_Cev, t * JOBS + L + 1)
                weigh(o[:, 0, :], 0, 0).then_inc(s_op, 1)
                pool.wait_ge(s_Cev, t * JOBS + L + 2)
                weigh(o[:, 1, :], 1, 0)
                link(weigh(rot[:, :], 1, 1))
                nc.gpsimd.tensor_tensor(o[:, 1, :], o[:, 1, :], rot[:, :], ALU.add).then_inc(s_op, 1)
                pool.wait_ge(s_ssq, t + 1)
                nc.gpsimd.tensor_tensor(ssq[:, 1, :], ssq[:, 0, :], mhalf[:, :], ALU.pow).then_inc(s_rstdo, 1)
                pool.wait_ge(s_rstdo, t + 1)
                for l in range(L):
                    ol = o[:, l, :].rearrange("p (h d) -> p h d", h=H)
                    nc.gpsimd.tensor_tensor(ol, ol, ssq[:, 1, l * H:(l + 1) * H].unsqueeze(2).broadcast_to([P, H, HDV]),
                                            ALU.mult).then_inc(s_on, 1)
                if not last:
                    for k in range(K):
                        y_lo(t + 1, k)

        @block.tensor
        def _(pe):
            pe.wait_ge(s_small, 16 * 5)
            pe.wait_ge(s_am, 1)
            nc.tensor.transpose(psD[0:2, 0:P], am2[:, :], ident[:, :]).then_inc(s_amT, 1)
            pe.wait_ge(s_diag, 1)
            nc.tensor.matmul(psD[:, 0:2], ones2[:, :], g2[:, 2:4], start=True, stop=True).then_inc(s_amB, 1)

            def a_transposes(t, l):
                n = t * L + l
                pe.wait_ge(s_q, L * K + n + 1)
                if l >= 2:
                    pe.wait_ge(s_xqT, n - 1)
                elif t == 1:
                    pe.wait_ge(s_cv, K)
                elif t >= 2:
                    pe.wait_ge(s_zl, (t - 1) * K)
                dst = psT[n % 2][:, 0:K * P // 2].bitcast(bf16)
                for k in range(K):
                    ins = nc.tensor.transpose(dst[:, k * P:(k + 1) * P], xq[:, n % 2, k * P:(k + 1) * P], ident16[:, :])
                ins.then_inc(s_AT, 1)

            def a_product(t, l):
                n = t * L + l
                pe.wait_ge(s_xqT, n + 1)
                if l >= 2:
                    pe.wait_ge(s_x1, n - 1)
                elif t >= 2:
                    pe.wait_ge(s_out, (t - 1) * L)
                for k in range(K):
                    ins = nc.tensor.matmul(psO[n % 2][:, :], xqT[:, n % 2, k, :], CQ[:, l * K + k, :],
                                           start=k == 0, stop=k == K - 1)
                ins.then_inc(s_AO, 1)

            def stage_a(t):
                a_transposes(t, 0)
                for l in range(L):
                    if l + 1 < L:
                        a_transposes(t, l + 1)
                    a_product(t, l)

            def stage_b(t):
                pe.wait_ge(s_xn2, (t + 1) * L)
                pe.wait_ge(s_xqT, (t + 1) * L)
                for k in range(K):
                    if k >= 2:
                        pe.wait_ge(s_cv, t * K + k - 1)
                    for l in range(L):
                        ins = nc.tensor.transpose(psT[k % 2][:, l * P:(l + 1) * P], stage[:, l, k * P:(k + 1) * P], ident[:, :])
                    ins.then_inc(s_BT, 1)

            def three(dst, a_h, a_l, w_h, w_l):
                for k in range(K):
                    nc.tensor.matmul(dst, a_h(k), w_h[:, k, :], start=k == 0, stop=False)
                    nc.tensor.matmul(dst, a_h(k), w_l[:, k, :], start=False, stop=False)
                    ins = nc.tensor.matmul(dst, a_l(k), w_h[:, k, :], start=False, stop=k == K - 1)
                return ins

            def stage_c(t, c):
                w_h, w_l = ((Wqk_h, Wqk_l), (Wv_h, Wv_l), (Wg_h, Wg_l))[c]
                if c == 0:
                    pe.wait_ge(s_yl, (t + 1) * K)
                if t == 0:
                    pe.wait_ge(s_wlo, c + 1)
                if c == 1:
                    if t == 0:
                        pe.wait_ge(s_wrl, 1)
                        pe.wait_ge(s_scale, 1)
                    else:
                        pe.wait_ge(s_dif, t)
                    for l in range(L):
                        ins = three(psD[:, l * H:(l + 1) * H], lambda k: yh[:, k, l * P:(l + 1) * P],
                                    lambda k: yl[:, k, l * P:(l + 1) * P], Wr_h, Wr_l)
                    ins.then_inc(s_R, 1)
                for l in range(L):
                    n = t * JOBS + c * L + l
                    if n >= 3:
                        pe.wait_ge(s_Cev, n - 2)
                    a_h = lambda k: yh[:, k, l * P:(l + 1) * P]
                    a_l = lambda k: yl[:, k, l * P:(l + 1) * P]
                    three(psC[n % 3][:, :], a_h, a_l, w_h, w_l).then_inc(s_C, 1)

            def stage_d(t):
                pe.wait_ge(s_z, (t + 1) * L)
                last = t == T - 1
                for k in range(K):
                    if k >= 2:
                        pe.wait_ge(s_zl, t * K + k - 1)
                    elif not last:
                        pe.wait_ge(s_cv, (t + 1) * K + k + 3)
                    else:
                        pe.wait_ge(s_zl, t * K)
                    for l in range(L):
                        ins = nc.tensor.transpose(psT[k % 2][:, l * P:(l + 1) * P], o[:, l, k * P:(k + 1) * P], ident[:, :])
                    ins.then_inc(s_DT, 1)

            def stage_e(t):
                pe.wait_ge(s_zl, (t + 1) * K)
                for l in range(L):
                    n = t * L + l
                    if l >= 2:
                        pe.wait_ge(s_out, n - 1)
                    elif t < T - 1:
                        pe.wait_ge(s_x1, (t + 2) * L)
                    else:
                        pe.wait_ge(s_out, t * L)
                    three(psO[n % 2][:, :], lambda k: zh[:, k, l * P:(l + 1) * P],
                          lambda k: zl[:, k, l * P:(l + 1) * P], Wo_h, Wo_l).then_inc(s_EO, 1)

            pe.wait_ge(s_id16, 1)
            stage_a(0)
            stage_b(0)
            for t in range(T):
                last = t == T - 1
                stage_c(t, 0)
                if not last:
                    stage_a(t + 1)
                stage_c(t, 1)
                stage_c(t, 2)
                if not last:
                    stage_b(t + 1)
                if t == 0:
                    pe.wait_ge(s_wlo, 4)
                stage_d(t)
                stage_e(t)


_INS = ['x', 'ctx_2048', 'mask_Bx1xS2_ff0', 'L0_ffn_conv_w', 'L0_ffn_Wq', 'L0_ffn_Wk', 'L0_ffn_Wv',
        'L0_ffn_Wg', 'L0_ffn_router_w', 'L0_ffn_Wout']


def _constants(length, heads_dk):
    inv_freq = (1.0 / np.float32(10000.0) ** (np.arange(0, heads_dk, 2, dtype=np.float32) / np.float32(heads_dk))).astype(np.float32)
    freqs = np.arange(length, dtype=np.float32)[:, None] * inv_freq[None, :]
    cos, sin = np.cos(freqs).astype(np.float32), np.sin(freqs).astype(np.float32)
    rope = np.stack([np.concatenate([cos, cos], 1), np.concatenate([-sin, sin], 1)])[None]
    tril = np.tril(np.ones((length, length), np.float32)).reshape(1, -1)
    return {'ident': np.eye(128, dtype=np.float32), 'rope': rope.astype(np.float32), 'tril': tril}


def kernel(**inputs):
    import concourse.bacc as _bacc
    from concourse.bass_utils import run_bass_kernel_spmd as _run

    nc = _bacc.Bacc("TRN2", target_bir_lowering=False, num_devices=1)
    arrays, args = {}, []
    for name in _INS:
        arrays[f"in_{name}"] = np.ascontiguousarray(inputs[name])
    heads = inputs['L0_ffn_router_w'].shape[0]
    consts = _constants(inputs['x'].shape[0], inputs['L0_ffn_Wq'].shape[1] // heads)
    for name, a in consts.items():
        arrays[f"const_{name}"] = a
    for name, a in arrays.items():
        args.append(nc.dram_tensor(name, a.shape, mybir.dt.from_np(a.dtype), kind="ExternalInput").ap())
    shape = tuple(inputs['x'].shape)
    args.append(nc.dram_tensor("out_0", shape, mybir.dt.float32, kind="ExternalOutput").ap())
    xattn_ffn_kernel(nc, *args)
    r = _run(nc, [arrays], core_ids=[0])
    return r.results[0]["out_0"]
```
